# Optimizing a Trainium2 kernel written in Bass

```python
import numpy as np
import jax
import jax.numpy as jnp

def _softmax(x, axis=-1):
    return jax.nn.softmax(x, axis=axis)

def _gelu(x):
    return jax.nn.gelu(x, approximate=True)

def _silu(x):
    return jax.nn.silu(x)

def _sigmoid(x):
    return jax.nn.sigmoid(x)

def _layernorm(x, axis=-1, eps=1e-05):
    m = jnp.mean(x, axis=axis, keepdims=True)
    v = jnp.var(x, axis=axis, keepdims=True)
    return (x - m) / jnp.sqrt(v + eps)

def _scatter_add(tgt, idx, src, axis=0):
    return tgt.at[idx].add(src)

def _segment_sum(src, seg, n):
    return jax.ops.segment_sum(src, seg, n)
kernel_name = 'mk_dlrm_tower_d1_rec_r8_ce2d71'

def setup_inputs(seed: int=0):
    np.random.seed(seed)
    _w = jnp.asarray

    def _rec_inputs():
        import jax
        import jax.numpy as jnp
        _tk = jax.random.key(seed)
        dense_ctx = jax.random.normal(jax.random.fold_in(_tk, 190), (512, 16), jnp.float32)
        ids = jnp.stack([jax.random.randint(jax.random.fold_in(_tk, 200 + f), (512,), 0, v, jnp.int32) for f, v in enumerate([1000, 125000, 1250, 1250, 1250, 12500, 1000, 1000, 12500, 12500, 1000, 12500, 12500, 1000, 1000, 12500, 1250, 1000, 1250, 12500, 1250, 12500, 1250, 1250, 1250, 1250, 1250])], axis=1)
        tbl_0 = 0.05 * jax.random.normal(jax.random.fold_in(_tk, 500 + 0), (1000, 128), jnp.float32)
        tbl_1 = 0.05 * jax.random.normal(jax.random.fold_in(_tk, 500 + 1), (125000, 128), jnp.float32)
        tbl_2 = 0.05 * jax.random.normal(jax.random.fold_in(_tk, 500 + 2), (1250, 128), jnp.float32)
        tbl_3 = 0.05 * jax.random.normal(jax.random.fold_in(_tk, 500 + 3), (1250, 128), jnp.float32)
        tbl_4 = 0.05 * jax.random.normal(jax.random.fold_in(_tk, 500 + 4), (1250, 128), jnp.float32)
        tbl_5 = 0.05 * jax.random.normal(jax.random.fold_in(_tk, 500 + 5), (12500, 128), jnp.float32)
        tbl_6 = 0.05 * jax.random.normal(jax.random.fold_in(_tk, 500 + 6), (1000, 128), jnp.float32)
        tbl_7 = 0.05 * jax.random.normal(jax.random.fold_in(_tk, 500 + 7), (1000, 128), jnp.float32)
        tbl_8 = 0.05 * jax.random.normal(jax.random.fold_in(_tk, 500 + 8), (12500, 128), jnp.float32)
        tbl_9 = 0.05 * jax.random.normal(jax.random.fold_in(_tk, 500 + 9), (12500, 128), jnp.float32)
        tbl_10 = 0.05 * jax.random.normal(jax.random.fold_in(_tk, 500 + 10), (1000, 128), jnp.float32)
        tbl_11 = 0.05 * jax.random.normal(jax.random.fold_in(_tk, 500 + 11), (12500, 128), jnp.float32)
        tbl_12 = 0.05 * jax.random.normal(jax.random.fold_in(_tk, 500 + 12), (12500, 128), jnp.float32)
        tbl_13 = 0.05 * jax.random.normal(jax.random.fold_in(_tk, 500 + 13), (1000, 128), jnp.float32)
        tbl_14 = 0.05 * jax.random.normal(jax.random.fold_in(_tk, 500 + 14), (1000, 128), jnp.float32)
        tbl_15 = 0.05 * jax.random.normal(jax.random.fold_in(_tk, 500 + 15), (12500, 128), jnp.float32)
        tbl_16 = 0.05 * jax.random.normal(jax.random.fold_in(_tk, 500 + 16), (1250, 128), jnp.float32)
        tbl_17 = 0.05 * jax.random.normal(jax.random.fold_in(_tk, 500 + 17), (1000, 128), jnp.float32)
        tbl_18 = 0.05 * jax.random.normal(jax.random.fold_in(_tk, 500 + 18), (1250, 128), jnp.float32)
        tbl_19 = 0.05 * jax.random.normal(jax.random.fold_in(_tk, 500 + 19), (12500, 128), jnp.float32)
        tbl_20 = 0.05 * jax.random.normal(jax.random.fold_in(_tk, 500 + 20), (1250, 128), jnp.float32)
        tbl_21 = 0.05 * jax.random.normal(jax.random.fold_in(_tk, 500 + 21), (12500, 128), jnp.float32)
        tbl_22 = 0.05 * jax.random.normal(jax.random.fold_in(_tk, 500 + 22), (1250, 128), jnp.float32)
        tbl_23 = 0.05 * jax.random.normal(jax.random.fold_in(_tk, 500 + 23), (1250, 128), jnp.float32)
        tbl_24 = 0.05 * jax.random.normal(jax.random.fold_in(_tk, 500 + 24), (1250, 128), jnp.float32)
        tbl_25 = 0.05 * jax.random.normal(jax.random.fold_in(_tk, 500 + 25), (1250, 128), jnp.float32)
        tbl_26 = 0.05 * jax.random.normal(jax.random.fold_in(_tk, 500 + 26), (1250, 128), jnp.float32)
        _rk = jax.random.fold_in(_tk, 7)
        W_top1 = 0.0521996 * jax.random.normal(jax.random.fold_in(_tk, 801), (367, 512), jnp.float32)
        W_top2 = 0.0441942 * jax.random.normal(jax.random.fold_in(_tk, 802), (512, 256), jnp.float32)
        W_top3 = 0.0625 * jax.random.normal(jax.random.fold_in(_tk, 803), (256, 1), jnp.float32)
        b_top1 = jnp.zeros((512,), jnp.float32)
        b_top2 = jnp.zeros((256,), jnp.float32)
        return (dense_ctx, ids, tbl_0, tbl_1, tbl_2, tbl_3, tbl_4, tbl_5, tbl_6, tbl_7, tbl_8, tbl_9, tbl_10, tbl_11, tbl_12, tbl_13, tbl_14, tbl_15, tbl_16, tbl_17, tbl_18, tbl_19, tbl_20, tbl_21, tbl_22, tbl_23, tbl_24, tbl_25, tbl_26, W_top1, b_top1, W_top2, b_top2, W_top3)
    dense_ctx, ids, tbl_0, tbl_1, tbl_2, tbl_3, tbl_4, tbl_5, tbl_6, tbl_7, tbl_8, tbl_9, tbl_10, tbl_11, tbl_12, tbl_13, tbl_14, tbl_15, tbl_16, tbl_17, tbl_18, tbl_19, tbl_20, tbl_21, tbl_22, tbl_23, tbl_24, tbl_25, tbl_26, W_top1, b_top1, W_top2, b_top2, W_top3 = _rec_inputs()

    def _L0_rec_setup():
        import jax, jax.numpy as jnp
        import numpy as np
        NUM_FEATURES = 27
        EMBED_DIM = 128
        BATCH = 4096
        key = jax.random.key(seed)
        inputs = jax.random.normal(key, (BATCH, NUM_FEATURES, EMBED_DIM), dtype=jnp.float32)
        return {'inputs': inputs}
    _L0_rec_all = _L0_rec_setup()
    _L0_rec_in = {k: v for k, v in _L0_rec_all.items() if k in ()}
    del _L0_rec_all
    return {'dense_ctx': dense_ctx, 'ids': ids, 'tbl_0': tbl_0, 'tbl_1': tbl_1, 'tbl_2': tbl_2, 'tbl_3': tbl_3, 'tbl_4': tbl_4, 'tbl_5': tbl_5, 'tbl_6': tbl_6, 'tbl_7': tbl_7, 'tbl_8': tbl_8, 'tbl_9': tbl_9, 'tbl_10': tbl_10, 'tbl_11': tbl_11, 'tbl_12': tbl_12, 'tbl_13': tbl_13, 'tbl_14': tbl_14, 'tbl_15': tbl_15, 'tbl_16': tbl_16, 'tbl_17': tbl_17, 'tbl_18': tbl_18, 'tbl_19': tbl_19, 'tbl_20': tbl_20, 'tbl_21': tbl_21, 'tbl_22': tbl_22, 'tbl_23': tbl_23, 'tbl_24': tbl_24, 'tbl_25': tbl_25, 'tbl_26': tbl_26, 'W_top1': W_top1, 'b_top1': b_top1, 'W_top2': W_top2, 'b_top2': b_top2, 'W_top3': W_top3}

def reference(dense_ctx, ids, tbl_0, tbl_1, tbl_2, tbl_3, tbl_4, tbl_5, tbl_6, tbl_7, tbl_8, tbl_9, tbl_10, tbl_11, tbl_12, tbl_13, tbl_14, tbl_15, tbl_16, tbl_17, tbl_18, tbl_19, tbl_20, tbl_21, tbl_22, tbl_23, tbl_24, tbl_25, tbl_26, W_top1, b_top1, W_top2, b_top2, W_top3):
    import jax
    import jax.numpy as jnp

    def _L0_rec_ref(inputs):
        import jax, jax.numpy as jnp
        import numpy as np
        NUM_FEATURES = 27
        EMBED_DIM = 128
        BATCH = 4096
        interactions = jnp.einsum('bnd,bmd->bnm', inputs, inputs)
        n = inputs.shape[1]
        i, j = jnp.triu_indices(n, k=1)
        return interactions[:, i, j]
    e = jnp.stack([tbl_0[ids[:, 0]], tbl_1[ids[:, 1]], tbl_2[ids[:, 2]], tbl_3[ids[:, 3]], tbl_4[ids[:, 4]], tbl_5[ids[:, 5]], tbl_6[ids[:, 6]], tbl_7[ids[:, 7]], tbl_8[ids[:, 8]], tbl_9[ids[:, 9]], tbl_10[ids[:, 10]], tbl_11[ids[:, 11]], tbl_12[ids[:, 12]], tbl_13[ids[:, 13]], tbl_14[ids[:, 14]], tbl_15[ids[:, 15]], tbl_16[ids[:, 16]], tbl_17[ids[:, 17]], tbl_18[ids[:, 18]], tbl_19[ids[:, 19]], tbl_20[ids[:, 20]], tbl_21[ids[:, 21]], tbl_22[ids[:, 22]], tbl_23[ids[:, 23]], tbl_24[ids[:, 24]], tbl_25[ids[:, 25]], tbl_26[ids[:, 26]]], axis=1)
    z = _L0_rec_ref(e)
    z = z.reshape(z.shape[0], -1)
    h = jnp.concatenate([z, dense_ctx], axis=1)
    h = jnp.maximum(h @ W_top1 + b_top1, 0.0)
    h = jnp.maximum(h @ W_top2 + b_top2, 0.0)
    y = h @ W_top3
    return y

_drawn_inputs = setup_inputs


def setup_inputs(seed=0):
    import zlib

    import numpy as np

    out = dict(_drawn_inputs(seed))
    spreads = {'b_top1': (0.0, 0.1), 'b_top2': (0.0, 0.1)}
    factors = {}
    for name, (base, spread) in spreads.items():
        noise = np.random.default_rng([zlib.crc32(name.encode()), seed]).standard_normal(out[name].shape)
        drawn = base * np.exp(spread * noise) if base else spread * noise
        out[name] = jnp.asarray(drawn.astype(out[name].dtype))
    for name, factor in factors.items():
        out[name] = (out[name] * factor).astype(out[name].dtype)
    return out
```

```python
import concourse.bass as bass
from concourse import mybir
from contextlib import ExitStack

VOCAB = [1000, 125000, 1250, 1250, 1250, 12500, 1000, 1000, 12500, 12500, 1000, 12500, 12500, 1000, 1000,
         12500, 1250, 1000, 1250, 12500, 1250, 12500, 1250, 1250, 1250, 1250, 1250]
NF = len(VOCAB)
P = 128
BATCH = 512
BT = BATCH // P
FP = 32
S = 4
NG = P // S
JQ = 4
NC = (NF + JQ - 1) // JQ
JW = NC * JQ
ROW0 = [2 * c * (c + 1) for c in range(NC + 1)]
ZR = ROW0[NC]
DENSE = 16
H1, H2 = 512, 256
M1, M2 = H1 // P, H2 // P

ONEHOT_ROWS = 1000
ONEHOT = [f for f in range(NF) if VOCAB[f] == ONEHOT_ROWS]
KT = 8
KP = ONEHOT_ROWS // KT
GATHER = [f for f in range(NF) if f not in ONEHOT]
NO, NGA = len(ONEHOT), len(GATHER)
ORDER = GATHER + ONEHOT
CH = 4
CHUNKS = [list(range(a, min(a + CH, NGA))) for a in range(0, NGA, CH)]
NCH = len(CHUNKS)
RING = 4
RAW = 3
DOT_SETS = 4


def tower(nc, tables, gather_ids, onehot_ids, selectors, row_ids, identity, dense_t, w1, b1, w2, b2, w3, y):
    fp32, fp32r, fp16, i32 = mybir.dt.float32, mybir.dt.float32r, mybir.dt.float16, mybir.dt.int32
    ALU = mybir.AluOpType
    ACT = mybir.ActivationFunctionType

    with ExitStack() as ctx:
        def sb(name, shape, dt):
            return ctx.enter_context(nc.sbuf_tensor(name, shape, dt))

        def sem(name):
            return ctx.enter_context(nc.semaphore(name))

        ids_sb = sb("ids_sb", [P, BT, NF], i32)
        ohids_i = sb("ohids_i", [NO, BATCH], i32)
        ohids = sb("ohids", [NO, BATCH], fp16)
        sel = sb("sel", [NO, NO, P], fp16)
        rowid = sb("rowid", [P, KT], fp32)
        ident = sb("ident", [P, P], fp32)
        w1_sb = sb("w1_sb", [P, JQ, H1], fp32)
        b1_sb = sb("b1_sb", [P, M1], fp32)
        w2_sb = sb("w2_sb", [P, M1, H2], fp32)
        b2_sb = sb("b2_sb", [P, M2], fp32)
        w3_sb = sb("w3_sb", [P, M2], fp32)
        rows = sb("rows", [P, BT, NGA, P], fp32)
        rowsT = sb("rowsT", [P, BATCH, FP], fp32)
        raw = sb("raw", [KP, RAW, KT * P], fp32)
        top = sb("top", [KP, 2, KT * P], fp32r)
        low = sb("low", [KP, 2, KT * P], fp32r)
        hot = sb("hot", [KP, RING, BATCH], fp32r)
        dots = sb("dots", [P, BT, JW, NG], fp32)
        dotsQ = sb("dotsQ", [P, BT, S, ZR], fp32)
        dotsT = sb("dotsT", [P, JQ, BATCH], fp32)
        h1 = sb("h1", [P, M1, BATCH], fp32)
        h2 = sb("h2", [P, M2, BATCH], fp32)
        y_sb = sb("y_sb", [1, BATCH], fp32)

        ps = ctx.enter_context(nc.psum_tensor("ps", [P, 8, 512], fp32))
        TR = [0, 1]
        ACC = [2, 3]
        IDB = [4, 5]
        Q0, Q1 = 6, 7

        ids_in = sem("ids_in")
        onehot_consts_in = sem("onehot_consts_in")
        ident_in = sem("ident_in")
        mlp_in = sem("mlp_in")
        raw_in = [sem(f"raw_in{t}") for t in range(NO)]
        rows_in = [[sem(f"rows_in{b}_{c}") for c in range(NCH)] for b in range(BT)]
        pads_zero = sem("pads_zero")
        ohids_ready = sem("ohids_ready")
        idb_ready = sem("idb_ready")
        top_ready = sem("top_ready")
        low_ready = sem("low_ready")
        hot_ready = sem("hot_ready")
        hot_used = sem("hot_used")
        acc_ready = sem("acc_ready")
        acc_stored = sem("acc_stored")
        tr_ready = sem("tr_ready")
        tr_stored = sem("tr_stored")
        dots_ready = sem("dots_ready")
        dots_stored_dve = sem("dots_stored_dve")
        dots_stored_act = sem("dots_stored_act")
        q_ready = sem("q_ready")
        q_stored = sem("q_stored")
        z_ready = sem("z_ready")
        z_stored = sem("z_stored")
        h1_ready = sem("h1_ready")
        h1_stored = sem("h1_stored")
        h2_ready = sem("h2_ready")
        h2_stored = sem("h2_stored")
        y_ready = sem("y_ready")
        y_stored = sem("y_stored")
        y_out = sem("y_out")

        block = ctx.enter_context(nc.Block())

        @block.sync
        def _(sp):
            sp.dma_start(ids_sb[:], gather_ids).then_inc(ids_in, 16)
            sp.dma_start(ohids_i[:], onehot_ids).then_inc(onehot_consts_in, 16)
            sp.dma_start(sel[:], selectors).then_inc(onehot_consts_in, 16)
            sp.dma_start(rowid[:], row_ids).then_inc(onehot_consts_in, 16)

            def load_table(t):
                src = tables[ONEHOT[t]].rearrange("(p k) d -> p (k d)", k=KT)
                for a, b in ((0, 120), (120, KP)):
                    sp.dma_start(raw[a:b, t % RAW, :], src[a:b, :]).then_inc(raw_in[t], 16)

            for t in range(min(RAW, NO)):
                load_table(t)
                if t == 0:
                    sp.dma_start(ident[:], identity).then_inc(ident_in, 16)
            for t in range(RAW, NO):
                sp.wait_ge(low_ready, t - RAW + 1)
                load_table(t)
            for dst, src in ((w1_sb[:], w1), (b1_sb[:], b1), (w2_sb[:], w2), (b2_sb[:], b2), (w3_sb[:], w3),
                             (dotsT[ZR:P, 0, :], dense_t)):
                sp.dma_start(dst, src).then_inc(mlp_in, 16)
            sp.wait_ge(y_stored, BT)
            sp.dma_start(y, y_sb[:]).then_inc(y_out, 16)
            sp.wait_ge(y_out, 16)

        @block.gpsimd
        def _(pool):
            pool.wait_ge(ids_in, 16)
            for b in range(BT):
                for c, chunk in enumerate(CHUNKS):
                    for n in chunk:
                        f = GATHER[n]
                        nc.gpsimd.indirect_dma_start(
                            out=rows[:, b, n, :], out_offset=None, in_=tables[f],
                            in_offset=bass.IndirectOffsetOnAxis(ap=ids_sb[:, b, f:f + 1], axis=0),
                        ).then_inc(rows_in[b][c], 16)

        early = {t: t - 2 for t in range(2, NO) if t - 2 < NCH}

        @block.tensor
        def _(pe):
            def transpose_rows(b, c):
                i = b * NCH + c
                pe.wait_ge(rows_in[b][c], 16 * len(CHUNKS[c]))
                if i >= 2:
                    pe.wait_ge(tr_stored, i - 1)
                for u, n in enumerate(CHUNKS[c]):
                    last = nc.tensor.transpose(ps[:, TR[i % 2], u * P:(u + 1) * P], rows[:, b, n, :], ident[:])
                last.then_inc(tr_ready, 1)

            def spread_ids(t):
                if t >= 2:
                    pe.wait_ge(hot_ready, (t - 1) * KT)
                nc.tensor.matmul(ps[:, IDB[t % 2], :], sel[:, t, :], ohids[:], start=True,
                                 stop=True).then_inc(idb_ready, 1)

            def look_up(t):
                pe.wait_ge(top_ready, t + 1)
                pe.wait_ge(low_ready, t + 1)
                if t >= 2:
                    pe.wait_ge(acc_stored, t - 1)
                for k in range(KT):
                    pe.wait_ge(hot_ready, t * KT + k + 1)
                    i = t * KT + k
                    for part, w in enumerate((top, low)):
                        last = nc.tensor.matmul(ps[:, ACC[t % 2], :], w[:, t % 2, k * P:(k + 1) * P],
                                                hot[:, i % RING, :], start=(k == 0 and part == 0),
                                                stop=(k == KT - 1 and part == 1))
                    last.then_inc(hot_used, 1)

            pe.wait_ge(onehot_consts_in, 48)
            pe.wait_ge(ohids_ready, 1)
            spread_ids(0)
            done = set()
            for t in range(NO):
                if t + 1 < NO:
                    spread_ids(t + 1)
                look_up(t)
                if t in early:
                    if not done:
                        pe.wait_ge(ident_in, 16)
                    transpose_rows(0, early[t])
                    done.add(early[t])

            pe.wait_ge(pads_zero, 1)
            for b in range(BT):
                for c in range(NCH):
                    if b or c not in done:
                        transpose_rows(b, c)
                pe.wait_ge(tr_stored, (b + 1) * NCH)
                if b == 0:
                    pe.wait_ge(acc_stored, NO)
                    pe.wait_ge(hot_ready, NO * KT)
                for h in range(DOT_SETS):
                    i = b * DOT_SETS + h
                    banks = (IDB, ACC)[i % 2]
                    if i >= 2:
                        pe.wait_ge(dots_stored_dve, i - 1)
                        pe.wait_ge(dots_stored_act, i - 1)
                    for g in range(8):
                        at = b * P + (h * 8 + g) * S
                        four = rowsT[:, at:at + S, :]
                        last = nc.tensor.matmul(
                            ps[:, banks[g // 4], (g % 4) * S * JW:(g % 4 + 1) * S * JW].rearrange(
                                "p (s j) -> p s j", s=S),
                            four.rearrange("p s f -> p (s f)"), four[:, :, 0:JW], start=True, stop=True)
                    last.then_inc(dots_ready, 1)
                pe.wait_ge(dots_stored_dve, (b + 1) * DOT_SETS)
                pe.wait_ge(dots_stored_act, (b + 1) * DOT_SETS)
                if b:
                    pe.wait_ge(y_stored, b)
                for c in range(NC):
                    last = nc.tensor.transpose(ps[:, (Q0, Q1)[c // 4], (c % 4) * P:(c % 4 + 1) * P],
                                               dots[:, b, c * JQ:(c + 1) * JQ, :].rearrange("p q g -> p (q g)"), ident[:])
                last.then_inc(q_ready, 1)
                pe.wait_ge(q_stored, b + 1)
                for s in range(S):
                    last = nc.tensor.transpose(ps[0:ZR, Q0, s * P:(s + 1) * P], dotsQ[:, b, s, :], ident[:])
                last.then_inc(z_ready, 1)
                pe.wait_ge(z_stored, b + 1)
                if b == 0:
                    pe.wait_ge(mlp_in, 96)
                cols = slice(b * P, (b + 1) * P)
                for m in range(M1):
                    for q in range(JQ):
                        k = P if q == 0 else ZR
                        last = nc.tensor.matmul(ps[:, Q1, m * P:(m + 1) * P], w1_sb[0:k, q, m * P:(m + 1) * P],
                                                dotsT[0:k, q, cols], start=(q == 0), stop=(q == JQ - 1))
                last.then_inc(h1_ready, 1)
                pe.wait_ge(h1_stored, b + 1)
                for m in range(M2):
                    for k in range(M1):
                        last = nc.tensor.matmul(ps[:, Q0, m * P:(m + 1) * P], w2_sb[:, k, m * P:(m + 1) * P],
                                                h1[:, k, cols], start=(k == 0), stop=(k == M1 - 1))
                last.then_inc(h2_ready, 1)
                pe.wait_ge(h2_stored, b + 1)
                for k in range(M2):
                    last = nc.tensor.matmul(ps[0:1, Q1, 0:P], w3_sb[:, k:k + 1], h2[:, k, cols],
                                            start=(k == 0), stop=(k == M2 - 1))
                last.then_inc(y_ready, 1)

        def store_dots(copy, b, h, lanes):
            banks = (IDB, ACC)[(b * DOT_SETS + h) % 2]
            for s in lanes:
                part = slice(s * FP, (s + 1) * FP)
                src = ps[part, banks[0]:banks[0] + 2, 0:4 * S * JW].rearrange(
                    "p k (g s j) -> p j k g s", g=4, s=S)[:, :, :, :, s]
                dst = dots[part, b, :, h * 8:(h + 1) * 8].rearrange("p j (k g) -> p j k g", k=2)
                last = copy(dst, src)
            return last

        @block.scalar
        def _(act):
            def take_top(t):
                act.wait_ge(raw_in[t], 32)
                if t >= 2:
                    act.wait_ge(hot_used, (t - 1) * KT)
                nc.scalar.copy(top[:, t % 2, :], raw[:, t % RAW, :]).then_inc(top_ready, 1)

            def store_look_up(t):
                act.wait_ge(hot_used, (t + 1) * KT)
                nc.scalar.copy(rowsT[:, :, NGA + t], ps[:, ACC[t % 2], :]).then_inc(acc_stored, 1)

            def store_rows(b, c):
                i = b * NCH + c
                act.wait_ge(tr_ready, i + 1)
                n, w = CHUNKS[c][0], len(CHUNKS[c])
                src = ps[:, TR[i % 2], 0:w * P].rearrange("p (f s) -> p s f", f=w)
                nc.scalar.copy(rowsT[:, b * P:(b + 1) * P, n:n + w], src).then_inc(tr_stored, 1)

            take_top(0)
            take_top(1)
            done = set()
            for t in range(NO):
                store_look_up(t)
                if t + 2 < NO:
                    take_top(t + 2)
                if t in early:
                    store_rows(0, early[t])
                    done.add(early[t])
            for b in range(BT):
                for c in range(NCH):
                    if b or c not in done:
                        store_rows(b, c)
                for h in range(DOT_SETS):
                    act.wait_ge(dots_ready, b * DOT_SETS + h + 1)
                    store_dots(nc.scalar.copy, b, h, (2, 3)).then_inc(dots_stored_act, 1)
                if b == 0:
                    act.wait_ge(mlp_in, 96)
                act.wait_ge(h1_ready, b + 1)
                for m in range(M1):
                    last = nc.scalar.activation(h1[:, m, b * P:(b + 1) * P], ps[:, Q1, m * P:(m + 1) * P],
                                                ACT.Relu, bias=b1_sb[:, m:m + 1])
                last.then_inc(h1_stored, 1)

        @block.vector
        def _(dve):
            nc.vector.memset(rowsT[:, :, NF:FP], 0.0).then_inc(pads_zero, 1)
            dve.wait_ge(onehot_consts_in, 48)
            nc.vector.tensor_copy(ohids[:], ohids_i[:]).then_inc(ohids_ready, 1)
            for t in range(NO):
                dve.wait_ge(top_ready, t + 1)
                nc.vector.tensor_tensor(low[:, t % 2, :], raw[:, t % RAW, :], top[:, t % 2, :],
                                        ALU.subtract).then_inc(low_ready, 1)
                dve.wait_ge(idb_ready, t + 1)
                for k in range(KT):
                    i = t * KT + k
                    if i >= RING:
                        dve.wait_ge(hot_used, i - RING + 1)
                    nc.vector.tensor_scalar(hot[:, i % RING, :], ps[0:KP, IDB[t % 2], :], rowid[0:KP, k:k + 1],
                                            None, ALU.is_equal).then_inc(hot_ready, 1)
            for b in range(BT):
                for h in range(DOT_SETS):
                    dve.wait_ge(dots_ready, b * DOT_SETS + h + 1)
                    store_dots(nc.vector.tensor_copy, b, h, (0, 1)).then_inc(dots_stored_dve, 1)
                dve.wait_ge(q_ready, b + 1)
                for c in range(NC):
                    src = ps[:, (Q0, Q1)[c // 4], (c % 4) * P:(c % 4 + 1) * P].rearrange("p (s i) -> p s i", s=S)
                    last = nc.vector.tensor_copy(dotsQ[:, b, :, ROW0[c]:ROW0[c + 1]], src[:, :, 0:4 * c + 4])
                last.then_inc(q_stored, 1)
                dve.wait_ge(z_ready, b + 1)
                for q in range(JQ):
                    src = ps[0:ZR, Q0, :].rearrange("p (s q g) -> p s q g", s=S, q=JQ)[:, :, q, :]
                    dst = dotsT[0:ZR, q, b * P:(b + 1) * P].rearrange("p (s g) -> p s g", s=S)
                    last = nc.vector.tensor_copy(dst, src)
                last.then_inc(z_stored, 1)
                if b == 0:
                    dve.wait_ge(mlp_in, 96)
                dve.wait_ge(h2_ready, b + 1)
                for m in range(M2):
                    last = nc.vector.tensor_scalar(h2[:, m, b * P:(b + 1) * P], ps[:, Q0, m * P:(m + 1) * P],
                                                   b2_sb[:, m:m + 1], 0.0, ALU.add, ALU.max)
                last.then_inc(h2_stored, 1)
                dve.wait_ge(y_ready, b + 1)
                nc.vector.tensor_copy(y_sb[:, b * P:(b + 1) * P], ps[0:1, Q1, 0:P]).then_inc(y_stored, 1)


def kernel(**inputs):
    import numpy as np
    import concourse.bacc as bacc
    from concourse.bass_utils import run_bass_kernel_spmd

    ids = np.asarray(inputs["ids"]).reshape(BT, S, NG, NF).transpose(2, 1, 0, 3).reshape(P, BT, NF)
    onehot_ids = ids[:, :, ONEHOT].transpose(2, 1, 0).reshape(NO, BATCH)
    w_top1 = np.asarray(inputs["W_top1"])
    w1 = np.zeros((P, JQ, H1), w_top1.dtype)
    for j in range(1, NF):
        for i in range(j):
            a, c = sorted((ORDER[i], ORDER[j]))
            w1[ROW0[j // JQ] + i, j % JQ] = w_top1[a * NF - a * (a + 1) // 2 + c - a - 1]
    w1[ZR:, 0] = w_top1[NF * (NF - 1) // 2:]
    selectors = np.zeros((NO, NO, P), np.float16)
    for t in range(NO):
        selectors[t, t] = 1
    args = {
        "gather_ids": ids,
        "onehot_ids": onehot_ids,
        "selectors": selectors,
        "row_ids": np.arange(P * KT, dtype=np.float32).reshape(P, KT),
        "identity": np.eye(P, dtype=np.float32),
        "dense_t": np.asarray(inputs["dense_ctx"]).T,
        "w1": w1,
        "b1": np.asarray(inputs["b_top1"]).reshape(M1, P).T,
        "w2": np.asarray(inputs["W_top2"]).reshape(M1, P, H2).transpose(1, 0, 2),
        "b2": np.asarray(inputs["b_top2"]).reshape(M2, P).T,
        "w3": np.asarray(inputs["W_top3"]).reshape(M2, P).T,
    }
    nc = bacc.Bacc("TRN2", target_bir_lowering=False, num_devices=1)
    arrays = {}

    def dram(name, a):
        arrays[name] = np.ascontiguousarray(a)
        return nc.dram_tensor(name, arrays[name].shape, mybir.dt.from_np(arrays[name].dtype), kind="ExternalInput").ap()

    tables = [dram(f"tbl_{f}", inputs[f"tbl_{f}"]) for f in range(NF)]
    args = {name: dram(name, a) for name, a in args.items()}
    y = nc.dram_tensor("y", (1, BATCH), mybir.dt.float32, kind="ExternalOutput").ap()
    tower(nc, tables, y=y, **args)
    r = run_bass_kernel_spmd(nc, [arrays], core_ids=[0])
    return r.results[0]["y"].reshape(BATCH, 1)
```

```python
import concourse.bass as bass
from concourse import mybir
from contextlib import ExitStack

VOCAB = [1000, 125000, 1250, 1250, 1250, 12500, 1000, 1000, 12500, 12500, 1000, 12500, 12500, 1000, 1000,
         12500, 1250, 1000, 1250, 12500, 1250, 12500, 1250, 1250, 1250, 1250, 1250]
NF = len(VOCAB)
P = 128
BATCH = 512
BT = BATCH // P
FP = 32
S = 4
NG = P // S
JQ = 4
NC = (NF + JQ - 1) // JQ
JW = NC * JQ
ROW0 = [2 * c * (c + 1) for c in range(NC + 1)]
ZR = ROW0[NC]
DENSE = 16
H1, H2 = 512, 256
M1, M2 = H1 // P, H2 // P

ONEHOT_ROWS = 1000
ONEHOT = [f for f in range(NF) if VOCAB[f] == ONEHOT_ROWS][:6]
KT = 8
KP = ONEHOT_ROWS // KT
GATHER = [f for f in range(NF) if f not in ONEHOT]
NO = len(ONEHOT)
NO0 = 4
ORDER = GATHER + ONEHOT[::-1]
NGA = [NF - NO0, NF - NO]
CH = 4
CHUNKS = [[list(range(a, min(a + CH, NGA[b // 2]))) for a in range(0, NGA[b // 2], CH)] for b in range(BT)]
CHUNK0 = [sum(len(CHUNKS[a]) for a in range(b)) for b in range(BT + 1)]
UNITS = [(0, t) for t in range(NO0)] + [(1, t) for t in range(NO)]
HALF = BATCH // 2
RING = 8
RAW = 2
SETS = 8
SQ = NG // SETS


def order():
    out = []
    chunk = 0
    for u in range(NO0):
        out.append(("look_up", u, 0))
        if u >= 2 and chunk < len(CHUNKS[0]):
            out.append(("rows", 0, chunk))
            chunk += 1
    out += [("rows", 0, c) for c in range(chunk, len(CHUNKS[0]))]
    units = [("look_up", u, 0) for u in range(NO0, len(UNITS))]
    for b in range(BT):
        chunks = [("rows", b + 1, c) for c in range(len(CHUNKS[b + 1]))] if b + 1 < BT else []
        out += [("dots", b, h) for h in range(SETS)]
        for stage in ("first", "second", "layer1", "layer2", "layer3"):
            if units and b < 2:
                out.append(units.pop(0))
            if chunks:
                out.append(chunks.pop(0))
            out.append((stage, b, 0))
        if b == 1:
            out += units
        out += chunks
    return out


ORDER_OF_STAGES = order()


def compare_ahead(stages):
    units = [x for x in stages if x[0] == "look_up"]
    out = [units[0]]
    for x in stages:
        if x[0] != "look_up":
            out.append(x)
        elif x != units[-1]:
            out.append(units[units.index(x) + 1])
    return out


def tower(nc, tables, gather_ids, onehot_ids, selectors, row_ids, identity, dense_t, w1, b1, w2, b2, w3, y):
    fp32, fp32r, fp16, i32 = mybir.dt.float32, mybir.dt.float32r, mybir.dt.float16, mybir.dt.int32
    ALU = mybir.AluOpType
    ACT = mybir.ActivationFunctionType

    with ExitStack() as ctx:
        def sb(name, shape, dt):
            return ctx.enter_context(nc.sbuf_tensor(name, shape, dt))

        def sem(name):
            return ctx.enter_context(nc.semaphore(name))

        ids_sb = sb("ids_sb", [P, BT, NF], i32)
        ohids_i = sb("ohids_i", [NO, BATCH], i32)
        ohids = sb("ohids", [NO, BATCH], fp16)
        sel = sb("sel", [NO, NO, P], fp16)
        rowid = sb("rowid", [P, KT], fp32)
        ident = sb("ident", [P, P], fp32)
        w1_sb = sb("w1_sb", [P, JQ, H1], fp32)
        b1_sb = sb("b1_sb", [P, M1], fp32)
        w2_sb = sb("w2_sb", [P, M1, H2], fp32)
        b2_sb = sb("b2_sb", [P, M2], fp32)
        w3_sb = sb("w3_sb", [P, M2], fp32)
        rows = sb("rows", [P, 2, NGA[0], P], fp32)
        rowsT = sb("rowsT", [P, BATCH, FP], fp32)
        raw = sb("raw", [KP, RAW, KT * P], fp32)
        top = sb("top", [KP, NO, KT * P], fp32r)
        low = sb("low", [KP, NO, KT * P], fp32r)
        hot = sb("hot", [KP, RING, HALF], fp32r)
        dots = sb("dots", [P, 2, JW, NG], fp32)
        dotsQ = sb("dotsQ", [P, 2, S, ZR], fp32)
        dotsT = sb("dotsT", [P, JQ, BATCH], fp32)
        h1 = sb("h1", [P, 2, M1, P], fp32)
        h2 = sb("h2", [P, 2, M2, P], fp32)
        y_sb = sb("y_sb", [1, BATCH], fp32)

        ps = ctx.enter_context(nc.psum_tensor("ps", [P, 8, 512], fp32))
        TR = [0, 1]
        DOT = [4, 5]
        Q0, Q1 = 6, 7

        def acc(u):
            return ps[:, Q1 if u < NO0 and u % 2 else 2, 0:HALF]

        def idb(u):
            return ps[:, Q0 if u < NO0 and u % 2 else 3, 0:HALF]

        def before(u):
            return u - 1 if u < NO0 else u

        ids_in = sem("ids_in")
        onehot_consts_in = sem("onehot_consts_in")
        ident_in = sem("ident_in")
        mlp_in = sem("mlp_in")
        raw_in = [sem(f"raw_in{t}") for t in range(NO)]
        rows_in = [[sem(f"rows_in{b}_{c}") for c in range(len(CHUNKS[b]))] for b in range(BT)]
        pads_zero = sem("pads_zero")
        ohids_ready = sem("ohids_ready")
        idb_ready = sem("idb_ready")
        top_ready = sem("top_ready")
        low_ready = sem("low_ready")
        hot_ready = sem("hot_ready")
        hot_used = sem("hot_used")
        acc_stored = sem("acc_stored")
        tr_ready = sem("tr_ready")
        tr_stored = sem("tr_stored")
        dots_ready = sem("dots_ready")
        dots_dve_stored = sem("dots_dve_stored")
        dots_act_stored = sem("dots_act_stored")
        q_ready = sem("q_ready")
        q_stored = sem("q_stored")
        z_ready = sem("z_ready")
        z_stored = sem("z_stored")
        h1_ready = sem("h1_ready")
        h1_stored = sem("h1_stored")
        h2_ready = sem("h2_ready")
        h2_stored = sem("h2_stored")
        y_ready = sem("y_ready")
        y_stored = sem("y_stored")
        y_out = sem("y_out")

        block = ctx.enter_context(nc.Block())

        @block.sync
        def _(sp):
            sp.dma_start(ids_sb[:], gather_ids).then_inc(ids_in, 16)
            sp.dma_start(ohids_i[:], onehot_ids).then_inc(onehot_consts_in, 16)
            sp.dma_start(sel[:], selectors).then_inc(onehot_consts_in, 16)

            def load_table(t):
                src = tables[ONEHOT[t]].rearrange("(p k) d -> p (k d)", k=KT)
                for a, b in ((0, 120), (120, KP)):
                    sp.dma_start(raw[a:b, t % RAW, :], src[a:b, :]).then_inc(raw_in[t], 16)

            load_table(0)
            sp.dma_start(rowid[:], row_ids).then_inc(onehot_consts_in, 16)
            load_table(1)
            sp.dma_start(ident[:], identity).then_inc(ident_in, 16)
            for t in range(RAW, NO):
                sp.wait_ge(low_ready, t - RAW + 1)
                load_table(t)
            for dst, src in ((w1_sb[:], w1), (b1_sb[:], b1), (w2_sb[:], w2), (b2_sb[:], b2), (w3_sb[:], w3),
                             (dotsT[ZR:P, 0, :], dense_t)):
                sp.dma_start(dst, src).then_inc(mlp_in, 16)
            sp.wait_ge(y_stored, BT)
            sp.dma_start(y, y_sb[:]).then_inc(y_out, 16)
            sp.wait_ge(y_out, 16)

        @block.gpsimd
        def _(pool):
            pool.wait_ge(ids_in, 16)
            for b in range(BT):
                for c, chunk in enumerate(CHUNKS[b]):
                    if b >= 2:
                        pool.wait_ge(tr_ready, CHUNK0[b - 2] + c + 1)
                    for n in chunk:
                        f = ORDER[n]
                        nc.gpsimd.indirect_dma_start(
                            out=rows[:, b % 2, n, :], out_offset=None, in_=tables[f],
                            in_offset=bass.IndirectOffsetOnAxis(ap=ids_sb[:, b, f:f + 1], axis=0),
                        ).then_inc(rows_in[b][c], 16)

        @block.tensor
        def _(pe):
            def spread_ids(u):
                half, t = UNITS[u]
                if u >= 2:
                    pe.wait_ge(hot_ready, before(u) * KT)
                nc.tensor.matmul(idb(u), sel[:, t, :], ohids[:, half * HALF:(half + 1) * HALF],
                                 start=True, stop=True).then_inc(idb_ready, 1)

            def look_up(u):
                half, t = UNITS[u]
                if u + 1 < len(UNITS):
                    spread_ids(u + 1)
                if half == 0 or t >= NO0:
                    pe.wait_ge(top_ready, t + 1)
                    pe.wait_ge(low_ready, t + 1)
                if u >= 2:
                    pe.wait_ge(acc_stored, before(u))
                for k in range(KT):
                    i = u * KT + k
                    pe.wait_ge(hot_ready, i + 1)
                    nc.tensor.matmul(acc(u), top[:, t, k * P:(k + 1) * P], hot[:, i % RING, :],
                                     start=(k == 0), stop=False)
                    nc.tensor.matmul(acc(u), low[:, t, k * P:(k + 1) * P], hot[:, i % RING, :],
                                     start=False, stop=(k == KT - 1)).then_inc(hot_used, 1)

            def transpose_rows(b, c):
                i = CHUNK0[b] + c
                if i == 0:
                    pe.wait_ge(ident_in, 16)
                pe.wait_ge(rows_in[b][c], 16 * len(CHUNKS[b][c]))
                if i >= 2:
                    pe.wait_ge(tr_stored, i - 1)
                for n, f in enumerate(CHUNKS[b][c]):
                    last = nc.tensor.transpose(ps[:, TR[i % 2], n * P:(n + 1) * P], rows[:, b % 2, f, :], ident[:])
                last.then_inc(tr_ready, 1)

            def multiply_rows(b, h):
                i = b * SETS + h
                if h == 0:
                    if b == 0:
                        pe.wait_ge(pads_zero, 1)
                    pe.wait_ge(tr_stored, CHUNK0[b + 1])
                    pe.wait_ge(acc_stored, len(UNITS) if b >= 2 else NO0)
                if i >= 2:
                    pe.wait_ge(dots_dve_stored, i - 1)
                    pe.wait_ge(dots_act_stored, i - 1)
                for g in range(SQ):
                    at = b * P + (h * SQ + g) * S
                    four = rowsT[:, at:at + S, :]
                    out = ps[:, DOT[i % 2], g * S * JW:(g + 1) * S * JW].rearrange("p (s j) -> p s j", s=S)
                    last = nc.tensor.matmul(out, four.rearrange("p s f -> p (s f)"), four[:, :, 0:JW],
                                            start=True, stop=True)
                last.then_inc(dots_ready, 1)

            def first_transposes(b):
                pe.wait_ge(dots_dve_stored, (b + 1) * SETS)
                pe.wait_ge(dots_act_stored, (b + 1) * SETS)
                if b:
                    pe.wait_ge(y_stored, b)
                for c in range(NC):
                    last = nc.tensor.transpose(ps[:, (Q0, Q1)[c // 4], (c % 4) * P:(c % 4 + 1) * P],
                                               dots[:, b % 2, c * JQ:(c + 1) * JQ, :].rearrange("p q g -> p (q g)"),
                                               ident[:])
                last.then_inc(q_ready, 1)

            def second_transposes(b):
                pe.wait_ge(q_stored, 2 * (b + 1))
                for s in range(S):
                    last = nc.tensor.transpose(ps[0:ZR, (Q0, Q1)[s // 2], (s % 2) * P:(s % 2 + 1) * P],
                                               dotsQ[:, b % 2, s, :], ident[:])
                last.then_inc(z_ready, 1)

            def layer1(b):
                pe.wait_ge(z_stored, 2 * (b + 1))
                if b == 0:
                    pe.wait_ge(mlp_in, 96)
                for m in range(M1):
                    for q in range(JQ):
                        k = P if q == 0 else ZR
                        last = nc.tensor.matmul(ps[:, (Q0, Q1)[m // 2], (m % 2) * P:(m % 2 + 1) * P], w1_sb[0:k, q, m * P:(m + 1) * P],
                                                dotsT[0:k, q, b * P:(b + 1) * P], start=(q == 0), stop=(q == JQ - 1))
                last.then_inc(h1_ready, 1)

            def layer2(b):
                pe.wait_ge(h1_stored, 2 * (b + 1))
                for m in range(M2):
                    for k in range(M1):
                        last = nc.tensor.matmul(ps[:, (Q0, Q1)[m], 0:P], w2_sb[:, k, m * P:(m + 1) * P],
                                                h1[:, b % 2, k, :], start=(k == 0), stop=(k == M1 - 1))
                last.then_inc(h2_ready, 1)

            def layer3(b):
                pe.wait_ge(h2_stored, 2 * (b + 1))
                for k in range(M2):
                    last = nc.tensor.matmul(ps[0:1, Q0, 0:P], w3_sb[:, k:k + 1], h2[:, b % 2, k, :],
                                            start=(k == 0), stop=(k == M2 - 1))
                last.then_inc(y_ready, 1)

            pe.wait_ge(onehot_consts_in, 48)
            pe.wait_ge(ohids_ready, 1)
            spread_ids(0)
            for stage, b, n in ORDER_OF_STAGES:
                if stage == "look_up":
                    look_up(b)
                elif stage == "rows":
                    transpose_rows(b, n)
                elif stage == "dots":
                    multiply_rows(b, n)
                elif stage == "first":
                    first_transposes(b)
                elif stage == "second":
                    second_transposes(b)
                elif stage == "layer1":
                    layer1(b)
                elif stage == "layer2":
                    layer2(b)
                else:
                    layer3(b)

        def store_dots(copy, b, h, lanes):
            for s in lanes:
                part = slice(s * FP, (s + 1) * FP)
                src = ps[part, DOT[(b * SETS + h) % 2], 0:SQ * S * JW].rearrange(
                    "p (g s j) -> p j g s", g=SQ, s=S)[:, :, :, s]
                last = copy(dots[part, b % 2, :, h * SQ:(h + 1) * SQ], src)
            return last

        def store_first(copy, b, sets):
            for c in sets:
                src = ps[:, (Q0, Q1)[c // 4], (c % 4) * P:(c % 4 + 1) * P].rearrange("p (s i) -> p s i", s=S)
                last = copy(dotsQ[:, b % 2, :, ROW0[c]:ROW0[c + 1]], src[:, :, 0:4 * c + 4])
            return last

        def store_second(copy, b, pair):
            src = ps[0:ZR, (Q0, Q1)[pair], 0:2 * P].rearrange("p (s q g) -> p q s g", s=2, q=JQ)
            dst = dotsT[0:ZR, :, b * P + pair * 2 * NG:b * P + (pair + 1) * 2 * NG]
            return copy(dst.rearrange("p q (s g) -> p q s g", s=2), src)

        @block.scalar
        def _(act):
            def take_top(t):
                act.wait_ge(raw_in[t], 32)
                nc.scalar.copy(top[:, t, :], raw[:, t % RAW, :]).then_inc(top_ready, 1)

            def look_up(u):
                half, t = UNITS[u]
                if u + 1 < NO:
                    take_top(u + 1)
                act.wait_ge(hot_used, (u + 1) * KT)
                nc.scalar.copy(rowsT[:, half * HALF:(half + 1) * HALF, NF - 1 - t], acc(u)).then_inc(acc_stored, 1)

            def store_rows(b, c):
                i = CHUNK0[b] + c
                act.wait_ge(tr_ready, i + 1)
                n, w = CHUNKS[b][c][0], len(CHUNKS[b][c])
                src = ps[:, TR[i % 2], 0:w * P].rearrange("p (f s) -> p s f", f=w)
                nc.scalar.copy(rowsT[:, b * P:(b + 1) * P, n:n + w], src).then_inc(tr_stored, 1)

            take_top(0)
            for stage, b, n in ORDER_OF_STAGES:
                if stage == "look_up":
                    look_up(b)
                elif stage == "rows":
                    store_rows(b, n)
                elif stage == "dots":
                    act.wait_ge(dots_ready, b * SETS + n + 1)
                    store_dots(nc.scalar.copy, b, n, (2, 3)).then_inc(dots_act_stored, 1)
                elif stage == "first":
                    act.wait_ge(q_ready, b + 1)
                    store_first(nc.scalar.copy, b, (4, 5, 6)).then_inc(q_stored, 1)
                elif stage == "second":
                    act.wait_ge(z_ready, b + 1)
                    store_second(nc.scalar.copy, b, 1).then_inc(z_stored, 1)
                elif stage == "layer1":
                    act.wait_ge(h1_ready, b + 1)
                    for m in (2, 3):
                        last = nc.scalar.activation(h1[:, b % 2, m, :], ps[:, Q1, (m - 2) * P:(m - 1) * P],
                                                    ACT.Relu, bias=b1_sb[:, m:m + 1])
                    last.then_inc(h1_stored, 1)
                elif stage == "layer2":
                    act.wait_ge(h2_ready, b + 1)
                    nc.scalar.activation(h2[:, b % 2, 1, :], ps[:, Q1, 0:P],
                                         ACT.Relu, bias=b2_sb[:, 1:2]).then_inc(h2_stored, 1)

        @block.vector
        def _(dve):
            def take_low(t):
                dve.wait_ge(top_ready, t + 1)
                nc.vector.tensor_tensor(low[:, t, :], raw[:, t % RAW, :], top[:, t, :],
                                        ALU.subtract).then_inc(low_ready, 1)

            def look_up(u):
                if u < NO:
                    take_low(u)
                dve.wait_ge(idb_ready, u + 1)
                for k in range(KT):
                    i = u * KT + k
                    if i >= RING:
                        dve.wait_ge(hot_used, i - RING + 1)
                    nc.vector.tensor_scalar(hot[:, i % RING, :], idb(u)[0:KP, :], rowid[0:KP, k:k + 1],
                                            None, ALU.is_equal).then_inc(hot_ready, 1)

            nc.vector.memset(rowsT[:, :, NF:FP], 0.0).then_inc(pads_zero, 1)
            dve.wait_ge(onehot_consts_in, 48)
            nc.vector.tensor_copy(ohids[:], ohids_i[:]).then_inc(ohids_ready, 1)
            for stage, b, n in compare_ahead(ORDER_OF_STAGES):
                if stage == "look_up":
                    look_up(b)
                elif stage == "dots":
                    dve.wait_ge(dots_ready, b * SETS + n + 1)
                    store_dots(nc.vector.tensor_copy, b, n, (0, 1)).then_inc(dots_dve_stored, 1)
                elif stage == "first":
                    dve.wait_ge(q_ready, b + 1)
                    store_first(nc.vector.tensor_copy, b, (0, 1, 2, 3)).then_inc(q_stored, 1)
                elif stage == "second":
                    dve.wait_ge(z_ready, b + 1)
                    store_second(nc.vector.tensor_copy, b, 0).then_inc(z_stored, 1)
                elif stage == "layer1":
                    dve.wait_ge(h1_ready, b + 1)
                    for m in (0, 1):
                        last = nc.vector.tensor_scalar(h1[:, b % 2, m, :], ps[:, Q0, m * P:(m + 1) * P],
                                                       b1_sb[:, m:m + 1], 0.0, ALU.add, ALU.max)
                    last.then_inc(h1_stored, 1)
                elif stage == "layer2":
                    dve.wait_ge(h2_ready, b + 1)
                    nc.vector.tensor_scalar(h2[:, b % 2, 0, :], ps[:, Q0, 0:P],
                                            b2_sb[:, 0:1], 0.0, ALU.add, ALU.max).then_inc(h2_stored, 1)
                elif stage == "layer3":
                    dve.wait_ge(y_ready, b + 1)
                    nc.vector.tensor_copy(y_sb[:, b * P:(b + 1) * P], ps[0:1, Q0, 0:P]).then_inc(y_stored, 1)


def kernel(**inputs):
    import numpy as np
    import concourse.bacc as bacc
    from concourse.bass_utils import run_bass_kernel_spmd

    ids = np.asarray(inputs["ids"]).reshape(BT, S, NG, NF).transpose(2, 1, 0, 3).reshape(P, BT, NF)
    onehot_ids = ids[:, :, ONEHOT].transpose(2, 1, 0).reshape(NO, BATCH)
    w_top1 = np.asarray(inputs["W_top1"])
    w1 = np.zeros((P, JQ, H1), w_top1.dtype)
    for j in range(1, NF):
        for i in range(j):
            a, c = sorted((ORDER[i], ORDER[j]))
            w1[ROW0[j // JQ] + i, j % JQ] = w_top1[a * NF - a * (a + 1) // 2 + c - a - 1]
    w1[ZR:, 0] = w_top1[NF * (NF - 1) // 2:]
    selectors = np.zeros((NO, NO, P), np.float16)
    for t in range(NO):
        selectors[t, t] = 1
    args = {
        "gather_ids": ids,
        "onehot_ids": onehot_ids,
        "selectors": selectors,
        "row_ids": np.arange(P * KT, dtype=np.float32).reshape(P, KT),
        "identity": np.eye(P, dtype=np.float32),
        "dense_t": np.asarray(inputs["dense_ctx"]).T,
        "w1": w1,
        "b1": np.asarray(inputs["b_top1"]).reshape(M1, P).T,
        "w2": np.asarray(inputs["W_top2"]).reshape(M1, P, H2).transpose(1, 0, 2),
        "b2": np.asarray(inputs["b_top2"]).reshape(M2, P).T,
        "w3": np.asarray(inputs["W_top3"]).reshape(M2, P).T,
    }
    nc = bacc.Bacc("TRN2", target_bir_lowering=False, num_devices=1)
    arrays = {}

    def dram(name, a):
        arrays[name] = np.ascontiguousarray(a)
        return nc.dram_tensor(name, arrays[name].shape, mybir.dt.from_np(arrays[name].dtype), kind="ExternalInput").ap()

    tables = [dram(f"tbl_{f}", inputs[f"tbl_{f}"]) for f in range(NF)]
    args = {name: dram(name, a) for name, a in args.items()}
    y = nc.dram_tensor("y", (1, BATCH), mybir.dt.float32, kind="ExternalOutput").ap()
    tower(nc, tables, y=y, **args)
    r = run_bass_kernel_spmd(nc, [arrays], core_ids=[0])
    return r.results[0]["y"].reshape(BATCH, 1)
```

```python
import concourse.bass as bass
from concourse import mybir
from contextlib import ExitStack

VOCAB = [1000, 125000, 1250, 1250, 1250, 12500, 1000, 1000, 12500, 12500, 1000, 12500, 12500, 1000, 1000,
         12500, 1250, 1000, 1250, 12500, 1250, 12500, 1250, 1250, 1250, 1250, 1250]
NF = len(VOCAB)
P = 128
BATCH = 512
BT = BATCH // P
FP = 32
S = 4
NG = P // S
JQ = 3
NC = NF // JQ
IN = NF - 1
WIDE = (S - 1) * FP + IN
NI = [min(JQ * (c + 1) - 1, IN) for c in range(NC)]
ROW0 = [sum(NI[:c]) for c in range(NC + 1)]
ZR = ROW0[NC]
DENSE = 16
DENSE_PRODUCTS = ((0, 0), (0, 1), (1, 0), (1, 1), (0, 2), (2, 0))
H1, H2 = 512, 256
M1, M2 = H1 // P, H2 // P

KP = 125
SMALL = [f for f in range(NF) if VOCAB[f] == 1000]
LARGER = [f for f in range(NF) if VOCAB[f] == 1250][:1]
ONEHOT = SMALL + LARGER
KT = [VOCAB[f] // KP for f in ONEHOT]
NO, NO0 = len(ONEHOT), len(SMALL)
TILE0 = [sum(KT[:t]) if t < NO0 else 2 * KT[0] * (t - NO0) for t in range(NO)]
GATHER = [f for f in range(NF) if f not in ONEHOT]
ORDER = GATHER + ONEHOT[::-1]
NGA = [NF - NO0, NF - NO]
CH = 4
CHUNKS = [[list(range(a, min(a + CH, NGA[b // 2]))) for a in range(0, NGA[b // 2], CH)] for b in range(BT)]
CHUNKS[-1][-1:] = [CHUNKS[-1][-1][:-1], CHUNKS[-1][-1][-1:]]
CHUNK0 = [sum(len(CHUNKS[a]) for a in range(b)) for b in range(BT + 1)]
UNITS = [(0, t) for t in range(NO0)] + [(1, t) for t in range(NO)]
HALF = BATCH // 2
KG = 2
GROUP0 = [sum(KT[t] // KG for _, t in UNITS[:u]) for u in range(len(UNITS) + 1)]
RING = 8
WARM = 13
AHEAD = 2
SPLIT_AT = [t - AHEAD if t < NO0 else NO0 + 2 * (t - NO0) + 4 for t in range(NO)]
ROWS = 6
RAW = 3
RAW_IDS = 5
LATE_IDS = 13
SETS = 8
SQ = NG // SETS
EARLY = 1
ALTERNATE = NO0 + EARLY
FILL = {
    0: dict(first=(1, 1, 0), second=(1, 1, 0), layer1=(1, 1, 0), layer2=(1, 2, 0), layer3=(0, 0, 1)),
    1: dict(first=(1, 1, 0), second=(1, 1, 0), layer1=(1, 1, 0), layer2=(0, 2, 0), layer3=(0, 0, 1)),
    2: dict(first=(0, 1, 0), second=(0, 1, 0), layer1=(0, 1, 0), layer2=(0, 1, 0), layer3=(0, 2, 0)),
    3: dict(first=(0, 0, 0), second=(0, 0, 0), layer1=(0, 0, 0), layer2=(0, 0, 0), layer3=(0, 0, 0)),
}


def order():
    units = [("look_up", u, 0) for u in range(len(UNITS))]
    chunks = [[("rows", b, c) for c in range(len(CHUNKS[b]))] for b in range(BT)] + [[]]

    def take(queue, n):
        taken = queue[:n]
        del queue[:n]
        return taken

    out = take(units, 2)
    while len(units) > NO:
        out += take(units, 1) + take(chunks[0], 1)
    for _ in range(EARLY):
        out += take(units, 1) + take(chunks[0], 1)
    out += chunks[0]
    sets = [[("dots", b, h) for h in range(SETS)] for b in range(BT)] + [[]]
    for b in range(BT):
        out += sets[b]
        for stage in ("first", "second", "layer1", "layer2", "layer3"):
            n_units, n_chunks, n_sets = FILL[b][stage]
            out += take(units, n_units) + take(chunks[b + 1], n_chunks) + take(sets[b + 1], n_sets)
            out.append((stage, b, 0))
        out += chunks[b + 1]
    assert not units
    return out


ORDER_OF_STAGES = order()


def count_before(kind, stage):
    return sum(x[0] == kind for x in ORDER_OF_STAGES[:ORDER_OF_STAGES.index(stage)])


def compare_ahead(stages):
    units = [x for x in stages if x[0] == "look_up"]
    out = [units[0]]
    for x in stages:
        if x[0] != "look_up":
            out.append(x)
        elif x != units[-1]:
            out.append(units[units.index(x) + 1])
    return out


def tower(nc, tables, gather_ids, onehot_ids, minus_first_rows, identity, dense_t, w_dense, w1, b1, w2, b2, w3, y):
    fp32, fp32r, fp16, i32 = mybir.dt.float32, mybir.dt.float32r, mybir.dt.float16, mybir.dt.int32
    bf16 = mybir.dt.bfloat16
    ALU = mybir.AluOpType
    ACT = mybir.ActivationFunctionType

    with ExitStack() as ctx:
        def sb(name, shape, dt):
            return ctx.enter_context(nc.sbuf_tensor(name, shape, dt))

        def sem(name):
            return ctx.enter_context(nc.semaphore(name))

        ids_sb = sb("ids_sb", [P, BT, NF], i32)
        ident = sb("ident", [P, P], fp32)
        minus_row0 = sb("minus_row0", [P, 2], fp32)
        warm = sb("warm", [P, BATCH], bf16)
        scratch = sb("scratch", [P, 1], bf16)
        w1_sb = sb("w1_sb", [ZR, JQ, H1], fp32)
        parts = sb("parts", [2 * DENSE, 3, BATCH], bf16)
        denseK = sb("denseK", [len(DENSE_PRODUCTS) * DENSE, BATCH], bf16)
        w_denseK = sb("w_denseK", [len(DENSE_PRODUCTS) * DENSE, H1], bf16)
        b1_sb = sb("b1_sb", [P, M1], fp32)
        w2_sb = sb("w2_sb", [P, M1, H2], fp32)
        b2_sb = sb("b2_sb", [P, M2], fp32)
        w3_sb = sb("w3_sb", [P, M2], fp32)
        rows = sb("rows", [P, ROWS, CH, P], fp32)
        rowsT = sb("rowsT", [P, BATCH, FP], fp32)
        raw = sb("raw", [KP, RAW, max(KT) * P], fp32)
        top = sb("top", [KP, sum(KT[:NO0]), P], fp32r)
        low = sb("low", [KP, sum(KT[:NO0]), P], fp32r)
        raw_ids = sb("raw_ids", [P, RAW_IDS, HALF], i32)
        ids_wide = sb("ids_wide", [KP, AHEAD + 1, HALF], fp16)
        hot = sb("hot", [KP, RING, KG, HALF], fp32r)
        dots = sb("dots", [WIDE, 2, NF, NG], fp32)
        dotsQ = sb("dotsQ", [JQ * NG, S, ZR], fp32)
        dotsT = sb("dotsT", [ZR, JQ, BATCH], fp32)
        dense = dotsT[0:2 * DENSE, 0, :]
        rest = dotsT[0:2 * DENSE, 1, :]
        h1 = sb("h1", [P, M1, P], fp32)
        h2 = sb("h2", [P, M2, P], fp32)
        y_sb = sb("y_sb", [1, BATCH], fp32)

        ps = ctx.enter_context(nc.psum_tensor("ps", [P, 8, 512], fp32))
        TR = [0, 1]
        DOT = [4, 5]
        Q0, Q1, Z0, Z1 = 6, 7, 2, 3
        FIRST = [(Q0, (8, 7, 6)), (Q1, (5, 4, 3)), (Z0, (2, 1)), (Z1, (0,))]
        HID = [Z0, Z1, Q0, Q1]

        def acc(u):
            return ps[:, DOT[0] if u >= ALTERNATE else Q1 if u % 2 else Z1, 0:HALF]

        ids_in = sem("ids_in")
        ident_in = sem("ident_in")
        row0_in = sem("row0_in")
        raw_ids_in = [sem(f"raw_ids_in{u}") for u in range(len(UNITS))]
        mlp_in = sem("mlp_in")
        dense_in = sem("dense_in")
        parts_ready = sem("parts_ready")
        denseK_in = sem("denseK_in")
        raw_in = [sem(f"raw_in{t}") for t in range(NO)]
        rows_in = [[sem(f"rows_in{b}_{c}") for c in range(len(CHUNKS[b]))] for b in range(BT)]
        warm_ready = sem("warm_ready")
        pads_zero = sem("pads_zero")
        ids_stored = sem("ids_stored")
        top_ready = sem("top_ready")
        low_ready = sem("low_ready")
        hot_ready = sem("hot_ready")
        hot_used = sem("hot_used")
        acc_stored = sem("acc_stored")
        tr_ready = sem("tr_ready")
        tr_stored = sem("tr_stored")
        dots_ready = sem("dots_ready")
        dots_dve_stored = sem("dots_dve_stored")
        dots_act_stored = sem("dots_act_stored")
        q_ready = sem("q_ready")
        q_dve_stored = sem("q_dve_stored")
        q_act_stored = sem("q_act_stored")
        z_ready = sem("z_ready")
        z_dve_stored = sem("z_dve_stored")
        z_act_stored = sem("z_act_stored")
        h1_ready = sem("h1_ready")
        h1_dve_stored = sem("h1_dve_stored")
        h1_act_stored = sem("h1_act_stored")
        h2_ready = sem("h2_ready")
        h2_dve_stored = sem("h2_dve_stored")
        h2_act_stored = sem("h2_act_stored")
        y_ready = sem("y_ready")
        y_stored = sem("y_stored")
        y_out = sem("y_out")

        def unit_ids(u):
            half, t = UNITS[u]
            return onehot_ids[t:t + 1, half * HALF:(half + 1) * HALF].broadcast_to([P, HALF])

        block = ctx.enter_context(nc.Block())

        @block.sync
        def _(sp):
            def load_ids(u):
                if u >= RAW_IDS:
                    sp.wait_ge(ids_stored, u - RAW_IDS + 1)
                sp.dma_start(raw_ids[:, u % RAW_IDS, :], unit_ids(u)).then_inc(raw_ids_in[u], 16)

            def load_table(t):
                src = tables[ONEHOT[t]].rearrange("(p k) d -> p (k d)", k=KT[t])
                for a, b in ((0, 120), (120, KP)):
                    sp.dma_start(raw[a:b, t % RAW, 0:KT[t] * P], src[a:b, :]).then_inc(raw_in[t], 16)

            sp.dma_start(ids_sb[:], gather_ids).then_inc(ids_in, 16)
            sp.dma_start(minus_row0[:], minus_first_rows).then_inc(row0_in, 16)
            load_table(0)
            for t in range(1, NO0):
                load_ids(t)
                if t >= RAW:
                    sp.wait_ge(low_ready, t - RAW + 1)
                load_table(t)
                if t == 1:
                    sp.dma_start(ident[:], identity).then_inc(ident_in, 16)
            sp.dma_start(dotsT[0:DENSE, 0, :], dense_t).then_inc(dense_in, 16)
            sp.dma_start(dotsT[DENSE:2 * DENSE, 0, :], w_dense).then_inc(dense_in, 16)
            for u in range(NO0, ALTERNATE + AHEAD):
                load_ids(u)
            sp.wait_ge(acc_stored, NO0)
            for u in range(ALTERNATE + AHEAD, LATE_IDS):
                load_ids(u)
            for q in range(JQ):
                sp.dma_start(w1_sb[:, q, :], w1[:, q, :]).then_inc(mlp_in, 16)
            for dst, src in ((b1_sb[:], b1), (w2_sb[:], w2), (b2_sb[:], b2), (w3_sb[:], w3)):
                sp.dma_start(dst, src).then_inc(mlp_in, 16)
            sp.wait_ge(parts_ready, 4)
            for n, (a, b) in enumerate(DENSE_PRODUCTS):
                rows_n = slice(n * DENSE, (n + 1) * DENSE)
                sp.dma_start(denseK[rows_n, :], parts[0:DENSE, a, :]).then_inc(denseK_in, 16)
                sp.dma_start(w_denseK[rows_n, :], parts[DENSE:2 * DENSE, b, :]).then_inc(denseK_in, 16)
            for t in range(NO0, NO):
                sp.wait_ge(low_ready, t - RAW + 1)
                load_table(t)
            for u in range(LATE_IDS, len(UNITS)):
                load_ids(u)
            sp.wait_ge(y_stored, BT)
            sp.dma_start(y, y_sb[:]).then_inc(y_out, 16)
            sp.wait_ge(y_out, 16)

        @block.gpsimd
        def _(pool):
            pool.wait_ge(ids_in, 16)
            for b in range(BT):
                for c, chunk in enumerate(CHUNKS[b]):
                    i = CHUNK0[b] + c
                    if i >= ROWS:
                        pool.wait_ge(tr_ready, i - ROWS + 1)
                    for k, n in enumerate(chunk):
                        f = ORDER[n]
                        nc.gpsimd.indirect_dma_start(
                            out=rows[:, i % ROWS, k, :], out_offset=None, in_=tables[f],
                            in_offset=bass.IndirectOffsetOnAxis(ap=ids_sb[:, b, f:f + 1], axis=0),
                        ).then_inc(rows_in[b][c], 16)

        @block.tensor
        def _(pe):
            def keep_warm(n):
                for _ in range(n):
                    nc.tensor.matmul(ps[:, DOT[0], :], warm[:, 0:P], warm[:], start=True, stop=True)

            def look_up(u):
                half, t = UNITS[u]
                if half == 0 or t >= NO0:
                    pe.wait_ge(top_ready, t + 1)
                    pe.wait_ge(low_ready, t + 1)
                if u < ALTERNATE:
                    if u >= 2:
                        pe.wait_ge(acc_stored, u - 1)
                else:
                    if u > ALTERNATE:
                        pe.wait_ge(acc_stored, u)
                    sets = count_before("dots", ("look_up", u, 0))
                    if sets:
                        pe.wait_ge(dots_dve_stored, (sets - 1) // 2 * 2 + 1)
                        pe.wait_ge(dots_act_stored, (sets - 1) // 2 * 2 + 1)
                for k in range(KT[t]):
                    i, n = GROUP0[u] + k // KG, k % KG
                    if n == 0:
                        pe.wait_ge(hot_ready, i + 1)
                    hot_k = hot[:, i % RING, n, :]
                    nc.tensor.matmul(acc(u), top[:, TILE0[t] + k, :], hot_k, start=(k == 0), stop=False)
                    last = nc.tensor.matmul(acc(u), low[:, TILE0[t] + k, :], hot_k, start=False,
                                            stop=(k == KT[t] - 1))
                    if n == KG - 1:
                        last.then_inc(hot_used, 1)

            def transpose_rows(b, c):
                i = CHUNK0[b] + c
                if i == 0:
                    pe.wait_ge(ident_in, 16)
                pe.wait_ge(rows_in[b][c], 16 * len(CHUNKS[b][c]))
                if i >= 2:
                    pe.wait_ge(tr_stored, i - 1)
                for n in range(len(CHUNKS[b][c])):
                    last = nc.tensor.transpose(ps[:, TR[i % 2], n * P:(n + 1) * P], rows[:, i % ROWS, n, :], ident[:])
                last.then_inc(tr_ready, 1)

            def multiply_rows(b, h):
                i = b * SETS + h
                if h == 0:
                    pe.wait_ge(pads_zero, 1)
                    pe.wait_ge(tr_stored, CHUNK0[b + 1])
                    pe.wait_ge(acc_stored, len(UNITS) if b >= 2 else NO0)
                units = count_before("look_up", ("dots", b, h))
                if i % 2 == 0 and units > ALTERNATE:
                    pe.wait_ge(acc_stored, units)
                if i >= 2:
                    pe.wait_ge(dots_dve_stored, i - 1)
                    pe.wait_ge(dots_act_stored, i - 1)
                for g in range(SQ):
                    at = b * P + (h * SQ + g) * S
                    four = rowsT[:, at:at + S, :]
                    out = ps[0:WIDE, DOT[i % 2], g * S * NF:(g + 1) * S * NF].rearrange("p (s j) -> p s j", s=S)
                    last = nc.tensor.matmul(out, four.rearrange("p s f -> p (s f)")[:, 0:WIDE], four[:, :, 0:NF],
                                            start=True, stop=True)
                last.then_inc(dots_ready, 1)

            def first_transposes(b):
                pe.wait_ge(dots_dve_stored, (b + 1) * SETS)
                pe.wait_ge(dots_act_stored, (b + 1) * SETS)
                if b:
                    pe.wait_ge(y_stored, b)
                for bank, sets in FIRST:
                    for n, c in enumerate(sets):
                        last = nc.tensor.transpose(ps[0:JQ * NG, bank, n * P:n * P + WIDE],
                                                   dots[:, b % 2, c * JQ:(c + 1) * JQ, :].rearrange("p q g -> p (q g)"),
                                                   ident[0:WIDE, 0:WIDE])
                    last.then_inc(q_ready, 1)

            def second_transposes(b):
                pe.wait_ge(q_dve_stored, b + 1)
                pe.wait_ge(q_act_stored, b + 1)
                for bank, pair in ((Q0, (0, 1)), (Q1, (2, 3))):
                    for n, s in enumerate(pair):
                        last = nc.tensor.transpose(ps[0:ZR, bank, n * JQ * NG:(n + 1) * JQ * NG],
                                                   dotsQ[:, s, :], ident[0:JQ * NG, 0:JQ * NG])
                    last.then_inc(z_ready, 1)

            def layer1(b):
                if b == 0:
                    pe.wait_ge(mlp_in, (JQ + 4) * 16)
                for m in range(M1):
                    for q in range(JQ):
                        if m == 0:
                            pe.wait_ge(z_dve_stored, JQ * b + q + 1)
                            pe.wait_ge(z_act_stored, JQ * b + q + 1)
                        nc.tensor.matmul(ps[:, HID[m], 0:P], w1_sb[:, q, m * P:(m + 1) * P],
                                         dotsT[:, q, b * P:(b + 1) * P], start=(q == 0), stop=False)
                    if b == 0 and m == 0:
                        pe.wait_ge(denseK_in, 2 * len(DENSE_PRODUCTS) * 16)
                    last = nc.tensor.matmul(ps[:, HID[m], 0:P], w_denseK[:, m * P:(m + 1) * P],
                                            denseK[:, b * P:(b + 1) * P], start=False, stop=True)
                    last.then_inc(h1_ready, 1)

            def layer2(b):
                seen = 0
                for m, k in ((0, 0), (0, 1), (0, 2), (1, 0), (0, 3), (1, 1), (1, 2), (1, 3)):
                    if k == seen:
                        pe.wait_ge((h1_dve_stored, h1_act_stored)[k % 2], 2 * b + k // 2 + 1)
                        seen += 1
                    last = nc.tensor.matmul(ps[:, HID[m], 0:P], w2_sb[:, k, m * P:(m + 1) * P],
                                            h1[:, k, :], start=(k == 0), stop=(k == M1 - 1))
                    if k == M1 - 1:
                        last.then_inc(h2_ready, 1)

            def layer3(b):
                for k in range(M2):
                    pe.wait_ge((h2_dve_stored, h2_act_stored)[k], b + 1)
                    last = nc.tensor.matmul(ps[0:1, Q0, 0:P], w3_sb[:, k:k + 1], h2[:, k, :],
                                            start=(k == 0), stop=(k == M2 - 1))
                last.then_inc(y_ready, 1)

            pe.wait_ge(warm_ready, 1)
            keep_warm(WARM)
            for stage, b, n in ORDER_OF_STAGES:
                if stage == "look_up":
                    look_up(b)
                elif stage == "rows":
                    transpose_rows(b, n)
                elif stage == "dots":
                    multiply_rows(b, n)
                elif stage == "first":
                    first_transposes(b)
                elif stage == "second":
                    second_transposes(b)
                elif stage == "layer1":
                    layer1(b)
                elif stage == "layer2":
                    layer2(b)
                else:
                    layer3(b)

        def store_dots(copy, b, h, lanes):
            for s in lanes:
                part = slice(s * FP, min((s + 1) * FP, WIDE))
                src = ps[part, DOT[(b * SETS + h) % 2], 0:SQ * S * NF].rearrange(
                    "p (g s j) -> p j g s", g=SQ, s=S)[:, :, :, s]
                last = copy(dots[part, b % 2, :, h * SQ:(h + 1) * SQ], src)
            return last

        def store_first(wait, copy, b, places):
            for place in places:
                bank, sets = FIRST[place]
                wait(q_ready, len(FIRST) * b + place + 1)
                for n, c in enumerate(sets):
                    src = ps[0:JQ * NG, bank, n * P:(n + 1) * P].rearrange("p (s i) -> p s i", s=S)
                    last = copy(dotsQ[:, :, ROW0[c]:ROW0[c + 1]], src[:, :, 0:NI[c]])
            return last

        def store_second(copy, b, pair, q):
            src = ps[0:ZR, (Q0, Q1)[pair], 0:2 * JQ * NG].rearrange("p (s q g) -> p q s g", s=2, q=JQ)
            dst = dotsT[0:ZR, :, b * P + pair * 2 * NG:b * P + (pair + 1) * 2 * NG]
            return copy(dst.rearrange("p q (s g) -> p q s g", s=2)[:, q], src[:, q])

        @block.scalar
        def _(act):
            def take_top(t):
                act.wait_ge(raw_in[t], 32)
                if t >= NO0:
                    act.wait_ge(hot_used, GROUP0[NO0 + 2 * (t - NO0) + 2])
                nc.scalar.copy(top[:, TILE0[t]:TILE0[t] + KT[t], :].rearrange("p k d -> p (k d)"),
                               raw[:, t % RAW, 0:KT[t] * P]).then_inc(top_ready, 1)

            def store_ids(u):
                act.wait_ge(raw_ids_in[u], 16)
                if u > AHEAD:
                    act.wait_ge(hot_ready, GROUP0[u - AHEAD])
                larger = UNITS[u][1] // NO0
                nc.scalar.activation(ids_wide[:, u % (AHEAD + 1), :], raw_ids[0:KP, u % RAW_IDS, :], ACT.Identity,
                                     bias=minus_row0[0:KP, larger:larger + 1]).then_inc(ids_stored, 1)

            def look_up(u):
                half, t = UNITS[u]
                if u + AHEAD < len(UNITS):
                    store_ids(u + AHEAD)
                for t_next in range(AHEAD, NO):
                    if SPLIT_AT[t_next] == u:
                        take_top(t_next)
                act.wait_ge(hot_used, GROUP0[u + 1])
                nc.scalar.copy(rowsT[:, half * HALF:(half + 1) * HALF, NF - 1 - t], acc(u)).then_inc(acc_stored, 1)

            def store_rows(b, c):
                i = CHUNK0[b] + c
                act.wait_ge(tr_ready, i + 1)
                n, w = CHUNKS[b][c][0], len(CHUNKS[b][c])
                src = ps[:, TR[i % 2], 0:w * P].rearrange("p (f s) -> p s f", f=w)
                nc.scalar.copy(rowsT[:, b * P:(b + 1) * P, n:n + w], src).then_inc(tr_stored, 1)

            act.dma_start(raw_ids[:, 0, :], unit_ids(0)).then_inc(raw_ids_in[0], 16)
            act.wait_ge(warm_ready, 1)
            nc.scalar.activation(scratch[:], warm[:, 0:1], ACT.Identity)
            act.wait_ge(row0_in, 16)
            for t in range(AHEAD):
                store_ids(t)
                take_top(t)
            for stage, b, n in ORDER_OF_STAGES:
                if stage == "look_up":
                    look_up(b)
                elif stage == "rows":
                    store_rows(b, n)
                elif stage == "dots":
                    act.wait_ge(dots_ready, b * SETS + n + 1)
                    store_dots(nc.scalar.copy, b, n, (2, 3)).then_inc(dots_act_stored, 1)
                elif stage == "first":
                    store_first(act.wait_ge, nc.scalar.copy, b, (1, 3)).then_inc(q_act_stored, 1)
                elif stage == "second":
                    act.wait_ge(z_ready, 2 * b + 2)
                    for q in range(JQ):
                        store_second(nc.scalar.copy, b, 1, q).then_inc(z_act_stored, 1)
                elif stage == "layer1":
                    for m in (1, 3):
                        act.wait_ge(h1_ready, M1 * b + m + 1)
                        nc.scalar.activation(h1[:, m, :], ps[:, HID[m], 0:P],
                                             ACT.Relu, bias=b1_sb[:, m:m + 1]).then_inc(h1_act_stored, 1)
                elif stage == "layer2":
                    act.wait_ge(h2_ready, M2 * b + 2)
                    nc.scalar.activation(h2[:, 1, :], ps[:, HID[1], 0:P],
                                         ACT.Relu, bias=b2_sb[:, 1:2]).then_inc(h2_act_stored, 1)

        @block.vector
        def _(dve):
            def take_low(t):
                dve.wait_ge(top_ready, t + 1)
                tiles = slice(TILE0[t], TILE0[t] + KT[t])
                nc.vector.tensor_tensor(low[:, tiles, :].rearrange("p k d -> p (k d)"), raw[:, t % RAW, 0:KT[t] * P],
                                        top[:, tiles, :].rearrange("p k d -> p (k d)"),
                                        ALU.subtract).then_inc(low_ready, 1)

            def split_dense(step):
                if step == 0:
                    dve.wait_ge(dense_in, 32)
                    last = nc.vector.tensor_copy(parts[:, 0, :], dense)
                else:
                    dve.wait_ge(parts_ready, step)
                if step == 1:
                    last = nc.vector.tensor_tensor(rest, dense, parts[:, 0, :], ALU.subtract)
                elif step == 2:
                    last = nc.vector.tensor_copy(parts[:, 1, :], rest)
                elif step == 3:
                    last = nc.vector.tensor_tensor(parts[:, 2, :], rest, parts[:, 1, :], ALU.subtract)
                last.then_inc(parts_ready, 1)

            def look_up(u):
                half, t = UNITS[u]
                if u >= 2 and (half == 0 or t >= NO0):
                    take_low(t)
                dve.wait_ge(ids_stored, u + 1)
                ids = ids_wide[:, u % (AHEAD + 1), :]
                for k in range(KT[t]):
                    i, n = GROUP0[u] + k // KG, k % KG
                    if n == 0 and i >= RING:
                        dve.wait_ge(hot_used, i - RING + 1)
                    last = nc.vector.tensor_scalar(hot[:, i % RING, n, :], ids, float(k), None,
                                                   ALU.is_equal)
                    if n == KG - 1:
                        last.then_inc(hot_ready, 1)
                if u < 2:
                    take_low(t)

            nc.vector.memset(warm[:], 0.0).then_inc(warm_ready, 1)
            nc.vector.memset(rowsT[:, :, NF:FP], 0.0).then_inc(pads_zero, 1)
            for stage, b, n in compare_ahead(ORDER_OF_STAGES):
                if stage == "look_up":
                    look_up(b)
                elif stage == "dots":
                    dve.wait_ge(dots_ready, b * SETS + n + 1)
                    store_dots(nc.vector.tensor_copy, b, n, (0, 1)).then_inc(dots_dve_stored, 1)
                    if b == 0 and n < 4:
                        split_dense(n)
                elif stage == "first":
                    store_first(dve.wait_ge, nc.vector.tensor_copy, b, (0, 2)).then_inc(q_dve_stored, 1)
                elif stage == "second":
                    dve.wait_ge(z_ready, 2 * b + 1)
                    for q in range(JQ):
                        store_second(nc.vector.tensor_copy, b, 0, q).then_inc(z_dve_stored, 1)
                elif stage == "layer1":
                    for m in (0, 2):
                        dve.wait_ge(h1_ready, M1 * b + m + 1)
                        nc.vector.tensor_scalar(h1[:, m, :], ps[:, HID[m], 0:P], b1_sb[:, m:m + 1], 0.0,
                                                ALU.add, ALU.max).then_inc(h1_dve_stored, 1)
                elif stage == "layer2":
                    dve.wait_ge(h2_ready, M2 * b + 1)
                    nc.vector.tensor_scalar(h2[:, 0, :], ps[:, HID[0], 0:P],
                                            b2_sb[:, 0:1], 0.0, ALU.add, ALU.max).then_inc(h2_dve_stored, 1)
                elif stage == "layer3":
                    dve.wait_ge(y_ready, b + 1)
                    nc.vector.tensor_copy(y_sb[:, b * P:(b + 1) * P], ps[0:1, Q0, 0:P]).then_inc(y_stored, 1)


def kernel(**inputs):
    import numpy as np
    import concourse.bacc as bacc
    from concourse.bass_utils import run_bass_kernel_spmd

    ids = np.asarray(inputs["ids"]).reshape(BT, S, NG, NF).transpose(2, 1, 0, 3).reshape(P, BT, NF)
    onehot_ids = ids[:, :, ONEHOT].transpose(2, 1, 0).reshape(NO, BATCH)
    w_top1 = np.asarray(inputs["W_top1"])
    w1 = np.zeros((ZR, JQ, H1), w_top1.dtype)
    for j in range(1, NF):
        for i in range(j):
            a, c = sorted((ORDER[i], ORDER[j]))
            w1[ROW0[j // JQ] + i, j % JQ] = w_top1[a * NF - a * (a + 1) // 2 + c - a - 1]
    args = {
        "gather_ids": ids,
        "onehot_ids": onehot_ids,
        "identity": np.eye(P, dtype=np.float32),
        "minus_first_rows": -np.outer(np.arange(P), (KT[0], KT[-1])).astype(np.float32),
        "dense_t": np.asarray(inputs["dense_ctx"]).T,
        "w_dense": w_top1[NF * (NF - 1) // 2:],
        "w1": w1,
        "b1": np.asarray(inputs["b_top1"]).reshape(M1, P).T,
        "w2": np.asarray(inputs["W_top2"]).reshape(M1, P, H2).transpose(1, 0, 2),
        "b2": np.asarray(inputs["b_top2"]).reshape(M2, P).T,
        "w3": np.asarray(inputs["W_top3"]).reshape(M2, P).T,
    }
    nc = bacc.Bacc("TRN2", target_bir_lowering=False, num_devices=1)
    arrays = {}

    def dram(name, a):
        arrays[name] = np.ascontiguousarray(a)
        return nc.dram_tensor(name, arrays[name].shape, mybir.dt.from_np(arrays[name].dtype), kind="ExternalInput").ap()

    tables = [dram(f"tbl_{f}", inputs[f"tbl_{f}"]) for f in range(NF)]
    args = {name: dram(name, a) for name, a in args.items()}
    y = nc.dram_tensor("y", (1, BATCH), mybir.dt.float32, kind="ExternalOutput").ap()
    tower(nc, tables, y=y, **args)
    r = run_bass_kernel_spmd(nc, [arrays], core_ids=[0])
    return r.results[0]["y"].reshape(BATCH, 1)
```
